# Optimizing a Trainium2 kernel written in Bass

```python
import numpy as np
import jax
import jax.numpy as jnp

def _softmax(x, axis=-1):
    return jax.nn.softmax(x, axis=axis)

def _gelu(x):
    return jax.nn.gelu(x, approximate=True)

def _silu(x):
    return jax.nn.silu(x)

def _sigmoid(x):
    return jax.nn.sigmoid(x)

def _layernorm(x, axis=-1, eps=1e-05):
    m = jnp.mean(x, axis=axis, keepdims=True)
    v = jnp.var(x, axis=axis, keepdims=True)
    return (x - m) / jnp.sqrt(v + eps)

def _scatter_add(tgt, idx, src, axis=0):
    return tgt.at[idx].add(src)

def _segment_sum(src, seg, n):
    return jax.ops.segment_sum(src, seg, n)
kernel_name = 'mk_dlrm_tower_d1_rec_r8_f0e18f'

def setup_inputs(seed: int=0):
    np.random.seed(seed)
    _w = jnp.asarray

    def _rec_inputs():
        import jax
        import jax.numpy as jnp
        _tk = jax.random.key(seed)
        dense_ctx = jax.random.normal(jax.random.fold_in(_tk, 190), (512, 16), jnp.float32)
        ids = jnp.stack([jax.random.randint(jax.random.fold_in(_tk, 200 + f), (512,), 0, v, jnp.int32) for f, v in enumerate([1250, 125000, 125000, 125000, 12500, 125000, 1000, 1250, 125000, 1000, 1000, 125000, 1250, 1250, 1250, 125000, 1000, 1000, 12500, 125000, 125000, 1250, 1250, 12500, 1250, 12500, 1000, 1000, 1000, 1250, 1250, 125000, 1250, 1250, 12500, 12500, 125000, 125000, 1250, 1000, 125000, 12500, 1000, 12500, 1000, 125000, 12500, 1250, 1250, 12500])], axis=1)
        tbl_0 = 0.05 * jax.random.normal(jax.random.fold_in(_tk, 500 + 0), (1250, 16), jnp.float32)
        tbl_1 = 0.05 * jax.random.normal(jax.random.fold_in(_tk, 500 + 1), (125000, 16), jnp.float32)
        tbl_2 = 0.05 * jax.random.normal(jax.random.fold_in(_tk, 500 + 2), (125000, 16), jnp.float32)
        tbl_3 = 0.05 * jax.random.normal(jax.random.fold_in(_tk, 500 + 3), (125000, 16), jnp.float32)
        tbl_4 = 0.05 * jax.random.normal(jax.random.fold_in(_tk, 500 + 4), (12500, 16), jnp.float32)
        tbl_5 = 0.05 * jax.random.normal(jax.random.fold_in(_tk, 500 + 5), (125000, 16), jnp.float32)
        tbl_6 = 0.05 * jax.random.normal(jax.random.fold_in(_tk, 500 + 6), (1000, 16), jnp.float32)
        tbl_7 = 0.05 * jax.random.normal(jax.random.fold_in(_tk, 500 + 7), (1250, 16), jnp.float32)
        tbl_8 = 0.05 * jax.random.normal(jax.random.fold_in(_tk, 500 + 8), (125000, 16), jnp.float32)
        tbl_9 = 0.05 * jax.random.normal(jax.random.fold_in(_tk, 500 + 9), (1000, 16), jnp.float32)
        tbl_10 = 0.05 * jax.random.normal(jax.random.fold_in(_tk, 500 + 10), (1000, 16), jnp.float32)
        tbl_11 = 0.05 * jax.random.normal(jax.random.fold_in(_tk, 500 + 11), (125000, 16), jnp.float32)
        tbl_12 = 0.05 * jax.random.normal(jax.random.fold_in(_tk, 500 + 12), (1250, 16), jnp.float32)
        tbl_13 = 0.05 * jax.random.normal(jax.random.fold_in(_tk, 500 + 13), (1250, 16), jnp.float32)
        tbl_14 = 0.05 * jax.random.normal(jax.random.fold_in(_tk, 500 + 14), (1250, 16), jnp.float32)
        tbl_15 = 0.05 * jax.random.normal(jax.random.fold_in(_tk, 500 + 15), (125000, 16), jnp.float32)
        tbl_16 = 0.05 * jax.random.normal(jax.random.fold_in(_tk, 500 + 16), (1000, 16), jnp.float32)
        tbl_17 = 0.05 * jax.random.normal(jax.random.fold_in(_tk, 500 + 17), (1000, 16), jnp.float32)
        tbl_18 = 0.05 * jax.random.normal(jax.random.fold_in(_tk, 500 + 18), (12500, 16), jnp.float32)
        tbl_19 = 0.05 * jax.random.normal(jax.random.fold_in(_tk, 500 + 19), (125000, 16), jnp.float32)
        tbl_20 = 0.05 * jax.random.normal(jax.random.fold_in(_tk, 500 + 20), (125000, 16), jnp.float32)
        tbl_21 = 0.05 * jax.random.normal(jax.random.fold_in(_tk, 500 + 21), (1250, 16), jnp.float32)
        tbl_22 = 0.05 * jax.random.normal(jax.random.fold_in(_tk, 500 + 22), (1250, 16), jnp.float32)
        tbl_23 = 0.05 * jax.random.normal(jax.random.fold_in(_tk, 500 + 23), (12500, 16), jnp.float32)
        tbl_24 = 0.05 * jax.random.normal(jax.random.fold_in(_tk, 500 + 24), (1250, 16), jnp.float32)
        tbl_25 = 0.05 * jax.random.normal(jax.random.fold_in(_tk, 500 + 25), (12500, 16), jnp.float32)
        tbl_26 = 0.05 * jax.random.normal(jax.random.fold_in(_tk, 500 + 26), (1000, 16), jnp.float32)
        tbl_27 = 0.05 * jax.random.normal(jax.random.fold_in(_tk, 500 + 27), (1000, 16), jnp.float32)
        tbl_28 = 0.05 * jax.random.normal(jax.random.fold_in(_tk, 500 + 28), (1000, 16), jnp.float32)
        tbl_29 = 0.05 * jax.random.normal(jax.random.fold_in(_tk, 500 + 29), (1250, 16), jnp.float32)
        tbl_30 = 0.05 * jax.random.normal(jax.random.fold_in(_tk, 500 + 30), (1250, 16), jnp.float32)
        tbl_31 = 0.05 * jax.random.normal(jax.random.fold_in(_tk, 500 + 31), (125000, 16), jnp.float32)
        tbl_32 = 0.05 * jax.random.normal(jax.random.fold_in(_tk, 500 + 32), (1250, 16), jnp.float32)
        tbl_33 = 0.05 * jax.random.normal(jax.random.fold_in(_tk, 500 + 33), (1250, 16), jnp.float32)
        tbl_34 = 0.05 * jax.random.normal(jax.random.fold_in(_tk, 500 + 34), (12500, 16), jnp.float32)
        tbl_35 = 0.05 * jax.random.normal(jax.random.fold_in(_tk, 500 + 35), (12500, 16), jnp.float32)
        tbl_36 = 0.05 * jax.random.normal(jax.random.fold_in(_tk, 500 + 36), (125000, 16), jnp.float32)
        tbl_37 = 0.05 * jax.random.normal(jax.random.fold_in(_tk, 500 + 37), (125000, 16), jnp.float32)
        tbl_38 = 0.05 * jax.random.normal(jax.random.fold_in(_tk, 500 + 38), (1250, 16), jnp.float32)
        tbl_39 = 0.05 * jax.random.normal(jax.random.fold_in(_tk, 500 + 39), (1000, 16), jnp.float32)
        tbl_40 = 0.05 * jax.random.normal(jax.random.fold_in(_tk, 500 + 40), (125000, 16), jnp.float32)
        tbl_41 = 0.05 * jax.random.normal(jax.random.fold_in(_tk, 500 + 41), (12500, 16), jnp.float32)
        tbl_42 = 0.05 * jax.random.normal(jax.random.fold_in(_tk, 500 + 42), (1000, 16), jnp.float32)
        tbl_43 = 0.05 * jax.random.normal(jax.random.fold_in(_tk, 500 + 43), (12500, 16), jnp.float32)
        tbl_44 = 0.05 * jax.random.normal(jax.random.fold_in(_tk, 500 + 44), (1000, 16), jnp.float32)
        tbl_45 = 0.05 * jax.random.normal(jax.random.fold_in(_tk, 500 + 45), (125000, 16), jnp.float32)
        tbl_46 = 0.05 * jax.random.normal(jax.random.fold_in(_tk, 500 + 46), (12500, 16), jnp.float32)
        tbl_47 = 0.05 * jax.random.normal(jax.random.fold_in(_tk, 500 + 47), (1250, 16), jnp.float32)
        tbl_48 = 0.05 * jax.random.normal(jax.random.fold_in(_tk, 500 + 48), (1250, 16), jnp.float32)
        tbl_49 = 0.05 * jax.random.normal(jax.random.fold_in(_tk, 500 + 49), (12500, 16), jnp.float32)
        _rk = jax.random.fold_in(_tk, 7)
        W_top1 = 0.0283866 * jax.random.normal(jax.random.fold_in(_tk, 801), (1241, 512), jnp.float32)
        W_top2 = 0.0441942 * jax.random.normal(jax.random.fold_in(_tk, 802), (512, 256), jnp.float32)
        W_top3 = 0.0625 * jax.random.normal(jax.random.fold_in(_tk, 803), (256, 1), jnp.float32)
        b_top1 = jnp.zeros((512,), jnp.float32)
        b_top2 = jnp.zeros((256,), jnp.float32)
        return (dense_ctx, ids, tbl_0, tbl_1, tbl_2, tbl_3, tbl_4, tbl_5, tbl_6, tbl_7, tbl_8, tbl_9, tbl_10, tbl_11, tbl_12, tbl_13, tbl_14, tbl_15, tbl_16, tbl_17, tbl_18, tbl_19, tbl_20, tbl_21, tbl_22, tbl_23, tbl_24, tbl_25, tbl_26, tbl_27, tbl_28, tbl_29, tbl_30, tbl_31, tbl_32, tbl_33, tbl_34, tbl_35, tbl_36, tbl_37, tbl_38, tbl_39, tbl_40, tbl_41, tbl_42, tbl_43, tbl_44, tbl_45, tbl_46, tbl_47, tbl_48, tbl_49, W_top1, b_top1, W_top2, b_top2, W_top3)
    dense_ctx, ids, tbl_0, tbl_1, tbl_2, tbl_3, tbl_4, tbl_5, tbl_6, tbl_7, tbl_8, tbl_9, tbl_10, tbl_11, tbl_12, tbl_13, tbl_14, tbl_15, tbl_16, tbl_17, tbl_18, tbl_19, tbl_20, tbl_21, tbl_22, tbl_23, tbl_24, tbl_25, tbl_26, tbl_27, tbl_28, tbl_29, tbl_30, tbl_31, tbl_32, tbl_33, tbl_34, tbl_35, tbl_36, tbl_37, tbl_38, tbl_39, tbl_40, tbl_41, tbl_42, tbl_43, tbl_44, tbl_45, tbl_46, tbl_47, tbl_48, tbl_49, W_top1, b_top1, W_top2, b_top2, W_top3 = _rec_inputs()

    def _L0_rec_setup():
        import jax, jax.numpy as jnp
        import numpy as np
        _NUM_FIELDS = 50
        _I_IDX, _J_IDX = np.triu_indices(_NUM_FIELDS, k=1)
        key = jax.random.key(seed)
        x = jax.random.normal(key, (2048, _NUM_FIELDS, 16), dtype=jnp.float32)
        return {'x': x}
    _L0_rec_all = _L0_rec_setup()
    _L0_rec_in = {k: v for k, v in _L0_rec_all.items() if k in ()}
    del _L0_rec_all
    return {'dense_ctx': dense_ctx, 'ids': ids, 'tbl_0': tbl_0, 'tbl_1': tbl_1, 'tbl_2': tbl_2, 'tbl_3': tbl_3, 'tbl_4': tbl_4, 'tbl_5': tbl_5, 'tbl_6': tbl_6, 'tbl_7': tbl_7, 'tbl_8': tbl_8, 'tbl_9': tbl_9, 'tbl_10': tbl_10, 'tbl_11': tbl_11, 'tbl_12': tbl_12, 'tbl_13': tbl_13, 'tbl_14': tbl_14, 'tbl_15': tbl_15, 'tbl_16': tbl_16, 'tbl_17': tbl_17, 'tbl_18': tbl_18, 'tbl_19': tbl_19, 'tbl_20': tbl_20, 'tbl_21': tbl_21, 'tbl_22': tbl_22, 'tbl_23': tbl_23, 'tbl_24': tbl_24, 'tbl_25': tbl_25, 'tbl_26': tbl_26, 'tbl_27': tbl_27, 'tbl_28': tbl_28, 'tbl_29': tbl_29, 'tbl_30': tbl_30, 'tbl_31': tbl_31, 'tbl_32': tbl_32, 'tbl_33': tbl_33, 'tbl_34': tbl_34, 'tbl_35': tbl_35, 'tbl_36': tbl_36, 'tbl_37': tbl_37, 'tbl_38': tbl_38, 'tbl_39': tbl_39, 'tbl_40': tbl_40, 'tbl_41': tbl_41, 'tbl_42': tbl_42, 'tbl_43': tbl_43, 'tbl_44': tbl_44, 'tbl_45': tbl_45, 'tbl_46': tbl_46, 'tbl_47': tbl_47, 'tbl_48': tbl_48, 'tbl_49': tbl_49, 'W_top1': W_top1, 'b_top1': b_top1, 'W_top2': W_top2, 'b_top2': b_top2, 'W_top3': W_top3}

def reference(dense_ctx, ids, tbl_0, tbl_1, tbl_2, tbl_3, tbl_4, tbl_5, tbl_6, tbl_7, tbl_8, tbl_9, tbl_10, tbl_11, tbl_12, tbl_13, tbl_14, tbl_15, tbl_16, tbl_17, tbl_18, tbl_19, tbl_20, tbl_21, tbl_22, tbl_23, tbl_24, tbl_25, tbl_26, tbl_27, tbl_28, tbl_29, tbl_30, tbl_31, tbl_32, tbl_33, tbl_34, tbl_35, tbl_36, tbl_37, tbl_38, tbl_39, tbl_40, tbl_41, tbl_42, tbl_43, tbl_44, tbl_45, tbl_46, tbl_47, tbl_48, tbl_49, W_top1, b_top1, W_top2, b_top2, W_top3):
    import jax
    import jax.numpy as jnp

    def _L0_rec_ref(x):
        import jax, jax.numpy as jnp
        import numpy as np
        _NUM_FIELDS = 50
        _I_IDX, _J_IDX = np.triu_indices(_NUM_FIELDS, k=1)
        gram = jnp.einsum('bid,bjd->bij', x, x)
        return gram[:, _I_IDX, _J_IDX]
    e = jnp.stack([tbl_0[ids[:, 0]], tbl_1[ids[:, 1]], tbl_2[ids[:, 2]], tbl_3[ids[:, 3]], tbl_4[ids[:, 4]], tbl_5[ids[:, 5]], tbl_6[ids[:, 6]], tbl_7[ids[:, 7]], tbl_8[ids[:, 8]], tbl_9[ids[:, 9]], tbl_10[ids[:, 10]], tbl_11[ids[:, 11]], tbl_12[ids[:, 12]], tbl_13[ids[:, 13]], tbl_14[ids[:, 14]], tbl_15[ids[:, 15]], tbl_16[ids[:, 16]], tbl_17[ids[:, 17]], tbl_18[ids[:, 18]], tbl_19[ids[:, 19]], tbl_20[ids[:, 20]], tbl_21[ids[:, 21]], tbl_22[ids[:, 22]], tbl_23[ids[:, 23]], tbl_24[ids[:, 24]], tbl_25[ids[:, 25]], tbl_26[ids[:, 26]], tbl_27[ids[:, 27]], tbl_28[ids[:, 28]], tbl_29[ids[:, 29]], tbl_30[ids[:, 30]], tbl_31[ids[:, 31]], tbl_32[ids[:, 32]], tbl_33[ids[:, 33]], tbl_34[ids[:, 34]], tbl_35[ids[:, 35]], tbl_36[ids[:, 36]], tbl_37[ids[:, 37]], tbl_38[ids[:, 38]], tbl_39[ids[:, 39]], tbl_40[ids[:, 40]], tbl_41[ids[:, 41]], tbl_42[ids[:, 42]], tbl_43[ids[:, 43]], tbl_44[ids[:, 44]], tbl_45[ids[:, 45]], tbl_46[ids[:, 46]], tbl_47[ids[:, 47]], tbl_48[ids[:, 48]], tbl_49[ids[:, 49]]], axis=1)
    z = _L0_rec_ref(e)
    z = z.reshape(z.shape[0], -1)
    h = jnp.concatenate([z, dense_ctx], axis=1)
    h = jnp.maximum(h @ W_top1 + b_top1, 0.0)
    h = jnp.maximum(h @ W_top2 + b_top2, 0.0)
    y = h @ W_top3
    return y

_drawn_inputs = setup_inputs


def setup_inputs(seed=0):
    import zlib

    import numpy as np

    out = dict(_drawn_inputs(seed))
    spreads = {'b_top1': (0.0, 0.1), 'b_top2': (0.0, 0.1)}
    factors = {'tbl_0': 5.47,
     'tbl_1': 4.897,
     'tbl_2': 4.37,
     'tbl_3': 4.44,
     'tbl_4': 4.58,
     'tbl_5': 4.837,
     'tbl_6': 4.315,
     'tbl_7': 4.59,
     'tbl_8': 4.895,
     'tbl_9': 4.638,
     'tbl_10': 4.604,
     'tbl_11': 4.541,
     'tbl_12': 4.307,
     'tbl_13': 4.873,
     'tbl_14': 4.717,
     'tbl_15': 4.489,
     'tbl_16': 4.89,
     'tbl_17': 4.095,
     'tbl_18': 4.721,
     'tbl_19': 5.069,
     'tbl_20': 4.494,
     'tbl_21': 4.711,
     'tbl_22': 4.774,
     'tbl_23': 5.031,
     'tbl_24': 4.527,
     'tbl_25': 4.565,
     'tbl_26': 4.634,
     'tbl_27': 5.207,
     'tbl_28': 4.58,
     'tbl_29': 4.836,
     'tbl_30': 4.932,
     'tbl_31': 5.642,
     'tbl_32': 5.038,
     'tbl_33': 4.625,
     'tbl_34': 5.383,
     'tbl_35': 4.492,
     'tbl_36': 4.617,
     'tbl_37': 4.506,
     'tbl_38': 4.659,
     'tbl_39': 4.278,
     'tbl_40': 4.789,
     'tbl_41': 5.145,
     'tbl_42': 4.726,
     'tbl_43': 4.671,
     'tbl_44': 4.854,
     'tbl_45': 4.564,
     'tbl_46': 4.642,
     'tbl_47': 4.179,
     'tbl_48': 4.746,
     'tbl_49': 4.822}
    for name, (base, spread) in spreads.items():
        noise = np.random.default_rng([zlib.crc32(name.encode()), seed]).standard_normal(out[name].shape)
        drawn = base * np.exp(spread * noise) if base else spread * noise
        out[name] = jnp.asarray(drawn.astype(out[name].dtype))
    for name, factor in factors.items():
        out[name] = (out[name] * factor).astype(out[name].dtype)
    return out
```

```python
from contextlib import ExitStack

import numpy as np

import concourse.bass as bass
from concourse import mybir

P = 128
B = 512
TILES = B // P
F = 50
D = 16
ROWS = [1250, 125000, 125000, 125000, 12500, 125000, 1000, 1250, 125000, 1000, 1000, 125000, 1250,
        1250, 1250, 125000, 1000, 1000, 12500, 125000, 125000, 1250, 1250, 12500, 1250, 12500, 1000,
        1000, 1000, 1250, 1250, 125000, 1250, 1250, 12500, 12500, 125000, 125000, 1250, 1000, 125000,
        12500, 1000, 12500, 1000, 125000, 12500, 1250, 1250, 12500]
R = 10
SMALL = [f for f in range(F) if ROWS[f] <= R * P]
LARGE = [f for f in range(F) if ROWS[f] > R * P]
SLOTS = SMALL + LARGE
NS = len(SMALL)
NL = len(LARGE)
H1 = 512
H2 = 256
Q = 4
QP = P // Q
HALF = QP // 2
SEG = 64
WIDE = F - 1 - QP
CH = WIDE
ELEN = F * 2 * D + D
JU = HALF // 2
UNITS = 2 * (Q // 2)
BC = 4
SC = 3
NBC = -(-NS // BC)
NSC = -(-NS // SC)
SMALL_UNITS = NBC + NSC
ROUND = 1.5 * 2 ** 23


def field_groups(size):
    return [(a, min(a + size, NS)) for a in range(0, NS, size)]


def build_tower(nc, ids, ids_t, ctx_t, w1, w2, b2, w3, ident_in, iota_in, out, *tables):
    f32 = mybir.dt.float32
    bf16 = mybir.dt.bfloat16
    i32 = mybir.dt.int32
    ALU = mybir.AluOpType
    ACT = mybir.ActivationFunctionType
    AX = mybir.AxisListType

    ctx = ExitStack()
    with ctx:
        def sb(name, shape, dt=f32):
            return ctx.enter_context(nc.sbuf_tensor(name, shape, dt))

        def ps(name, shape):
            return ctx.enter_context(nc.psum_tensor(name, shape, f32))

        def sem(name):
            return ctx.enter_context(nc.semaphore(name))

        ids_sb = sb("ids_sb", [P, TILES, F], i32)
        ids_t_sb = sb("ids_t_sb", [NS, B], i32)
        ident = sb("ident", [P, P])
        iota = sb("iota", [P, 1 + R])
        table = sb("table", [P, NS, R * D])
        w1_sb = sb("w1_sb", [P, CH, H1])
        w2_sb = sb("w2_sb", [P, H1 // P, H2])
        b2_sb = sb("b2_sb", [1, H2])
        w3_sb = sb("w3_sb", [P, H2])
        select = sb("select", [NS, NS, P], bf16)
        quot_f = sb("quot_f", [NS, B])
        quot_t = sb("quot_t", [NS, B], bf16)
        quot = sb("quot", [P, TILES, NS])
        rem = sb("rem", [P, TILES, NS])
        mask = sb("mask", [P, TILES, NS, R])
        onehot = sb("onehot", [P, 2, NS, P])
        picked = sb("picked", [P, SC, D, R])
        emb = sb("emb", [P, TILES, ELEN])
        cols = sb("cols", [P, HALF + QP, 2, SEG])
        mov = sb("mov", [P, HALF, F])
        z = sb("z", [P, 2, CH, P])
        ones = sb("ones", [1, P])
        h1 = sb("h1", [P, H1])
        h1t = sb("h1t", [P, H1 // P, P])
        h2w = sb("h2w", [P, H2])
        y = sb("y", [P, TILES])

        gram = ps("gram", [P, Q, 512])
        p1 = ps("p1", [P, H1])
        pt = ps("pt", [P, H1 // P, P])
        psm = ps("psm", [P, 2, 512])

        ids_loaded = sem("ids_loaded")
        ids_t_loaded = sem("ids_t_loaded")
        consts_loaded = sem("consts_loaded")
        tables_loaded = sem("tables_loaded")
        w1_loaded = sem("w1_loaded")
        w2_loaded = sem("w2_loaded")
        ctx_loaded = [sem(f"ctx_loaded{i}") for i in range(2)]
        gathered = [sem(f"gathered{t}") for t in range(TILES)]
        select_ready = sem("select_ready")
        quot_ready = sem("quot_ready")
        z_cleared = sem("z_cleared")
        small_made = sem("small_made")
        small_used = sem("small_used")
        cols_ready = sem("cols_ready")
        gram_made = sem("gram_made")
        z_low = sem("z_low")
        z_high = sem("z_high")
        z_used = sem("z_used")
        h1_ready = sem("h1_ready")
        h1t_made = sem("h1t_made")
        h1t_ready = sem("h1t_ready")
        p2_made = sem("p2_made")
        p2_used = sem("p2_used")
        y_ready = sem("y_ready")
        stored = sem("stored")
        dve_step = sem("dve_step")

        block = ctx.enter_context(nc.Block())

        emb_slots = [emb[:, t, D:].rearrange("p (s c) -> p s c", c=2 * D) for t in range(TILES)]

        def copy_unit(copy, t, u, h):
            r, qp = divmod(u, Q // 2)
            base = SEG * h
            zt = z[:, t % 2, :, :].rearrange("p c (q j) -> p q j c", q=Q)
            j0 = HALF * h + JU * r
            q = slice(2 * qp, 2 * qp + 2)
            g = gram[:, q, 0:JU * (F - 1)].rearrange("p q (j y) -> p q j y", j=JU)
            copy(zt[0:SEG, q, j0:j0 + JU, 0:WIDE], g[base:base + SEG, :, :, QP:QP + WIDE])
            copy(zt[SEG:SEG + QP, q, j0:j0 + JU, 0:QP // 2], g[base:base + QP, :, :, 0:QP:2])
            return copy(zt[SEG + QP:P, q, j0:j0 + JU, 0:QP // 2], g[base:base + QP, :, :, 1:QP:2])

        @block.sync
        def _(sp):
            sp.dma_start(ids_sb[:], ids).then_inc(ids_loaded, 16)
            sp.dma_start(ids_t_sb[:], ids_t).then_inc(ids_t_loaded, 16)
            sp.dma_start(iota[:], iota_in).then_inc(consts_loaded, 16)
            sp.dma_start(ident[:], ident_in).then_inc(consts_loaded, 16)
            for s in range(NS):
                k = ROWS[SLOTS[s]] // R
                sp.dma_start(table[0:k, s, :],
                             tables[s].rearrange("(k r) d -> k (r d)", r=R)).then_inc(tables_loaded, 16)
            sp.wait_ge(z_cleared, 1)
            for t in range(TILES):
                if t >= 2:
                    sp.wait_ge(z_used, t - 1)
                sp.dma_start(z[SEG:SEG + D, t % 2, CH - 1, :], ctx_t[:, t, :]).then_inc(ctx_loaded[t % 2], 16)
            sp.wait_ge(y_ready, TILES)
            sp.dma_start(out.rearrange("(p t) o -> p (t o)", t=TILES), y[:]).then_inc(stored, 16)
            sp.wait_ge(stored, 16)

        @block.gpsimd
        def _(pool):
            pool.wait_ge(ids_loaded, 16)
            for t in range(TILES):
                for s in range(NS, F):
                    nc.gpsimd.indirect_dma_start(
                        emb_slots[t][:, s, 0:D], None, tables[s],
                        bass.IndirectOffsetOnAxis(ap=ids_sb[:, t, s:s + 1], axis=0),
                    ).then_inc(gathered[t], 16)

        @block.scalar
        def _(act):
            act.dma_start(w1_sb[:], w1.rearrange("p (c n) -> p c n", c=CH)).then_inc(w1_loaded, 16)
            act.dma_start(w2_sb[:], w2.rearrange("(k p) n -> p k n", p=P)).then_inc(w2_loaded, 16)
            act.dma_start(b2_sb[:], b2).then_inc(w2_loaded, 16)
            act.dma_start(w3_sb[:], w3.to_broadcast([P, H2])).then_inc(w2_loaded, 16)
            act.wait_ge(consts_loaded, 32)
            nc.scalar.activation(select[:], ident[0:NS, 0:NS].unsqueeze(2).to_broadcast([NS, NS, P]),
                                 ACT.Copy).then_inc(select_ready, 1)
            for t in range(TILES):
                if t >= 2:
                    act.wait_ge(z_used, t - 1)
                for u in range(UNITS):
                    act.wait_ge(gram_made, UNITS * t + u + 1)
                    copy_unit(nc.scalar.copy, t, u, 0).then_inc(z_low, 1)
                act.wait_ge(z_used, t + 1)
                nc.scalar.activation(h1[:], p1[:], ACT.Relu).then_inc(h1_ready, 1)
                act.wait_ge(h1t_made, t + 1)
                nc.scalar.copy(h1t[:], pt[:]).then_inc(h1t_ready, 1)

        @block.vector
        def _(dve):
            steps = [0]

            def step(ins):
                steps[0] += 1
                ins.then_inc(dve_step, 1)
                dve.wait_ge(dve_step, steps[0])

            for t in range(TILES):
                strips = emb[:, t, 0:F * 2 * D].rearrange("p (s c) -> p s c", c=2 * D)
                nc.vector.memset(strips[:, :, 0:D], 0.0)
                nc.vector.memset(emb[:, t, F * 2 * D:ELEN], 0.0)
            nc.vector.memset(cols[:, :, :, F:SEG], 0.0)
            nc.vector.memset(ones[:], 1.0)
            step(nc.vector.memset(z[SEG:P, :, CH - 1, :], 0.0))
            nc.vector.memset(z[SEG + QP:SEG + QP + 1, :, CH - 1, :], 1.0).then_inc(z_cleared, 1)

            dve.wait_ge(ids_t_loaded, 16)
            step(nc.vector.tensor_scalar(quot_f[:], ids_t_sb[:], -(R - 1) / 2, 1.0 / R, ALU.add, ALU.mult))
            nc.vector.tensor_scalar(quot_t[:], quot_f[:], ROUND, -ROUND, ALU.add, ALU.add).then_inc(quot_ready, 1)
            dve.wait_ge(ids_loaded, 16)
            step(nc.vector.tensor_scalar(quot[:], ids_sb[:, :, 0:NS], -(R - 1) / 2, 1.0 / R, ALU.add, ALU.mult))
            step(nc.vector.tensor_scalar(quot[:], quot[:], ROUND, -ROUND, ALU.add, ALU.add))
            step(nc.vector.scalar_tensor_tensor(rem[:], quot[:], -float(R), ids_sb[:, :, 0:NS],
                                                ALU.mult, ALU.add))
            dve.wait_ge(consts_loaded, 32)
            for t in range(TILES):
                ins = nc.vector.tensor_tensor(mask[:, t], rem[:, t].unsqueeze(2).to_broadcast([P, NS, R]),
                                              iota[:, 1:1 + R].unsqueeze(1).to_broadcast([P, NS, R]),
                                              ALU.is_equal)
            step(ins)

            def small_tables(t):
                n = SMALL_UNITS * t
                for u, (a, b) in enumerate(field_groups(BC)):
                    dve.wait_ge(small_made, n + u + 1)
                    if t >= 2 and u == 0:
                        dve.wait_ge(small_made, SMALL_UNITS * (t - 1))
                    nc.vector.tensor_scalar(onehot[:, t % 2, a:b, :], psm[:, (n + u) % 2, 0:(b - a) * P]
                                            .rearrange("p (f b) -> p f b", b=P),
                                            iota[:, 0:1], None, ALU.is_equal).then_inc(small_used, 1)
                for u, (a, b) in enumerate(field_groups(SC)):
                    m = n + NBC + u
                    k = b - a
                    dve.wait_ge(small_made, m + 1)
                    rows = psm[:, m % 2, 0:k * R * D].rearrange("p (f r d) -> p f d r", r=R, d=D)
                    ins = nc.vector.tensor_tensor(picked[:, 0:k], rows,
                                                  mask[:, t, a:b, :].unsqueeze(2).to_broadcast([P, k, D, R]),
                                                  ALU.mult)
                    ins.then_inc(small_used, 1)
                    dve.wait_ge(small_used, m + 1)
                    step(nc.vector.tensor_reduce(emb_slots[t][:, a:b, 0:D], picked[:, 0:k], AX.X, ALU.add))

            def columns(t, a, b):
                for h in range(2):
                    src = emb[:, t, D * (1 - h) + 2 * D * a:D * (1 - h) + 2 * D * b]
                    first = HALF * (1 - h)
                    dst = cols[:, first:first + QP, h, a:b].rearrange("p j s -> p s j")
                    ins = nc.vector.transpose(dst, src.rearrange("p (s c) -> p s c", c=2 * D))
                step(ins)
                return nc.vector.tensor_tensor(mov[:, :, a:b], cols[:, HALF:QP, 0, a:b],
                                               cols[:, HALF:QP, 1, a:b], ALU.add)

            def last_layer(t):
                if t == 0:
                    dve.wait_ge(w2_loaded, 48)
                dve.wait_ge(p2_made, t + 1)
                nc.vector.scalar_tensor_tensor(h2w[:], p1[:, 0:H2], 0.0, w3_sb[:], ALU.max, ALU.mult,
                                               accum_out=y[:, t:t + 1]).then_inc(y_ready, 1)

            small_tables(0)
            small_tables(1)
            for t in range(TILES):
                if t >= 1:
                    dve.wait_ge(gram_made, UNITS * t)
                columns(t, 0, NS)
                dve.wait_ge(gathered[t], 16 * NL)
                columns(t, NS, F).then_inc(cols_ready, 1)
                if t >= 2:
                    dve.wait_ge(z_used, t - 1)
                for u in range(UNITS):
                    dve.wait_ge(gram_made, UNITS * t + u + 1)
                    copy_unit(nc.vector.tensor_copy, t, u, 1).then_inc(z_high, 1)
                if t + 2 < TILES:
                    small_tables(t + 2)
                last_layer(t)

        @block.tensor
        def _(pe):
            def small_steps(t):
                n = SMALL_UNITS * t
                for u, (a, b) in enumerate(field_groups(BC)):
                    if n + u >= 2:
                        pe.wait_ge(small_used, n + u - 1)
                    for f in range(a, b):
                        ins = nc.tensor.matmul(psm[:, (n + u) % 2, (f - a) * P:(f - a + 1) * P],
                                               select[:, f, :], quot_t[:, P * t:P * (t + 1)],
                                               start=True, stop=True)
                    ins.then_inc(small_made, 1)
                    yield
                for u, (a, b) in enumerate(field_groups(SC)):
                    m = n + NBC + u
                    pe.wait_ge(small_used, max(m - 1, n + -(-b // BC)))
                    for f in range(a, b):
                        k = ROWS[SLOTS[f]] // R
                        ins = nc.tensor.matmul(psm[:, m % 2, (f - a) * R * D:(f - a + 1) * R * D],
                                               onehot[0:k, t % 2, f, :], table[0:k, f, :],
                                               start=True, stop=True)
                    ins.then_inc(small_made, 1)
                    yield

            def gram_products(t):
                pe.wait_ge(cols_ready, t + 1)
                for u in range(UNITS):
                    r, qp = divmod(u, Q // 2)
                    if UNITS * t + u >= 2:
                        pe.wait_ge(z_low, UNITS * t + u - 1)
                        pe.wait_ge(z_high, UNITS * t + u - 1)
                    for jj in range(JU):
                        j = JU * r + jj
                        for q in (2 * qp, 2 * qp + 1):
                            rows = slice(QP * q, QP * (q + 1))
                            ins = nc.tensor.matmul(gram[:, q, jj * (F - 1):(jj + 1) * (F - 1)],
                                                   cols[rows, HALF + j, :, :].rearrange("p h s -> p (h s)"), mov[rows, j, 1:F],
                                                   start=True, stop=True)
                    ins.then_inc(gram_made, 1)

            def mlp(t, small):
                pe.wait_ge(z_low, UNITS * (t + 1))
                pe.wait_ge(z_high, UNITS * (t + 1))
                pe.wait_ge(ctx_loaded[t % 2], 16 * (t // 2 + 1))
                if t == 0:
                    pe.wait_ge(w1_loaded, 16)
                    pe.wait_ge(w2_loaded, 48)
                if t >= 1:
                    pe.wait_ge(y_ready, t)
                for c in range(CH):
                    ins = nc.tensor.matmul(p1[:], z[:, t % 2, c, :], w1_sb[:, c, :],
                                           start=(c == 0), stop=(c == CH - 1))
                    if c < CH - 1:
                        next(small, None)
                ins.then_inc(z_used, 1)
                for _ in small:
                    pass
                pe.wait_ge(h1_ready, t + 1)
                for k in range(H1 // P):
                    ins = nc.tensor.transpose(pt[:, k, :], h1[:, P * k:P * (k + 1)], ident[:])
                ins.then_inc(h1t_made, 1)
                nc.tensor.matmul(p1[:, 0:H2], ones[:], b2_sb[:], start=True, stop=False)
                pe.wait_ge(h1t_ready, t + 1)
                for k in range(H1 // P):
                    ins = nc.tensor.matmul(p1[:, 0:H2], h1t[:, k, :], w2_sb[:, k, :],
                                           start=False, stop=(k == H1 // P - 1))
                ins.then_inc(p2_made, 1)

            pe.wait_ge(select_ready, 1)
            pe.wait_ge(quot_ready, 1)
            pe.wait_ge(consts_loaded, 32)
            pe.wait_ge(z_cleared, 1)
            pe.wait_ge(tables_loaded, 16 * NS)
            for t in range(2):
                for _ in small_steps(t):
                    pass
            for t in range(TILES):
                gram_products(t)
                mlp(t, small_steps(t + 2) if t + 2 < TILES else iter(()))


def pair_index(i, j):
    return i * (2 * F - i - 1) // 2 + j - i - 1


def weight_rows():
    pairs = F * (F - 1) // 2
    bias, zero = pairs + D, pairs + D + 1
    rows = np.full((P, CH), zero)
    for yy in range(1, F):
        c, p0 = (yy - QP - 1, 0) if yy > QP else ((yy - 1) // 2, SEG + QP * ((yy - 1) % 2))
        for i in range(yy):
            a, b = sorted((SLOTS[i], SLOTS[yy]))
            rows[p0 + i, c] = pair_index(a, b)
    rows[SEG:SEG + D, CH - 1] = pairs + np.arange(D)
    rows[SEG + QP, CH - 1] = bias
    return rows


def kernel(**inputs):
    import concourse.bacc as bacc
    from concourse.bass_utils import run_bass_kernel_spmd

    a = {k: np.asarray(v) for k, v in inputs.items()}
    w1 = np.concatenate([a["W_top1"], a["b_top1"][None], np.zeros((1, H1), np.float32)])
    ids = a["ids"][:, SLOTS]
    arrays = {
        "ids": ids.reshape(P, TILES * F),
        "ids_t": ids[:, :NS].reshape(P, TILES, NS).transpose(2, 1, 0).reshape(NS, B),
        "ctx_t": a["dense_ctx"].reshape(P, TILES, D).transpose(2, 1, 0),
        "w1": w1[weight_rows()].reshape(P, CH * H1),
        "w2": a["W_top2"],
        "b2": a["b_top2"][None],
        "w3": a["W_top3"].reshape(1, H2),
        "ident": np.eye(P, dtype=np.float32),
        "iota": np.concatenate([np.arange(P)[:, None], np.tile(np.arange(R), (P, 1))], 1).astype(np.float32),
    }
    arrays = {f"in_{name}": np.ascontiguousarray(x) for name, x in arrays.items()}
    nc = bacc.Bacc("TRN2", target_bir_lowering=False, num_devices=1)
    args = []
    for name, x in arrays.items():
        args.append(nc.dram_tensor(name, x.shape, mybir.dt.from_np(x.dtype), kind="ExternalInput").ap())
    out = nc.dram_tensor("y_out", (B, 1), mybir.dt.float32, kind="ExternalOutput").ap()
    tabs = []
    for f in SLOTS:
        arrays[f"tbl_{f}"] = x = np.ascontiguousarray(a[f"tbl_{f}"])
        tabs.append(nc.dram_tensor(f"tbl_{f}", x.shape, mybir.dt.from_np(x.dtype), kind="ExternalInput").ap())
    args[0] = args[0].rearrange("p (t f) -> p t f", t=TILES)
    build_tower(nc, *args, out, *tabs)
    return run_bass_kernel_spmd(nc, [arrays], core_ids=[0]).results[0]["y_out"]
```

```python
import itertools
from contextlib import ExitStack

import numpy as np

import concourse.bass as bass
from concourse import mybir

P = 128
B = 512
TILES = B // P
F = 50
D = 16
ROWS = [1250, 125000, 125000, 125000, 12500, 125000, 1000, 1250, 125000, 1000, 1000, 125000, 1250,
        1250, 1250, 125000, 1000, 1000, 12500, 125000, 125000, 1250, 1250, 12500, 1250, 12500, 1000,
        1000, 1000, 1250, 1250, 125000, 1250, 1250, 12500, 12500, 125000, 125000, 1250, 1000, 125000,
        12500, 1000, 12500, 1000, 125000, 12500, 1250, 1250, 12500]
R = 10
SMALL = [f for f in range(F) if ROWS[f] <= R * P]
LARGE = [f for f in range(F) if ROWS[f] > R * P]
SLOTS = SMALL + LARGE
NS = len(SMALL)
NL = len(LARGE)
H1 = 512
H2 = 256
Q = 4
QP = P // Q
HALF = QP // 2
SEG = 64
WIDE = F - 1 - QP
CH = WIDE
JU = HALF // 2
UNITS = 2 * (Q // 2)
BC = 4
SC = 3
AHEAD = 3
LEAD = [0, 5, 5, 6]
NBC = -(-NS // BC)
NSC = -(-NS // SC)
ROUND = 1.5 * 2 ** 23


TABLE_PARTS = [(0, 2 * SC), (2 * SC, 5 * SC), (5 * SC, NS)]


def field_groups(size):
    return [(a, min(a + size, NS)) for a in range(0, NS, size)]


def broadcasts_sent(n):
    if n == 0:
        return 0
    t, u = divmod(n - 1, NSC)
    return min(NBC * TILES, NBC * t + -(-field_groups(SC)[u][1] // BC) + AHEAD)


def selections_sent(t, u):
    return min(NSC * TILES, NSC * (t + 2) + NSC * (u + 1) // UNITS)


def build_tower(nc, ids, ids_t, ctx_t, small, w1, w2, b2, w3, ident_in, iota_in, out, *tables):
    f32 = mybir.dt.float32
    bf16 = mybir.dt.bfloat16
    i32 = mybir.dt.int32
    ALU = mybir.AluOpType
    ACT = mybir.ActivationFunctionType
    AX = mybir.AxisListType

    ctx = ExitStack()
    with ctx:
        def sb(name, shape, dt=f32):
            return ctx.enter_context(nc.sbuf_tensor(name, shape, dt))

        def ps(name, shape):
            return ctx.enter_context(nc.psum_tensor(name, shape, f32))

        def sem(name):
            return ctx.enter_context(nc.semaphore(name))

        ids_sb = sb("ids_sb", [P, TILES, F], i32)
        ids_t_sb = sb("ids_t_sb", [NS, B], i32)
        ident = sb("ident", [P, P])
        iota = sb("iota", [P, 2 + R])
        table = sb("table", [P, NS, R * D])
        w1_sb = sb("w1_sb", [P, CH, H1])
        w2_sb = sb("w2_sb", [P, H1 // P, H2])
        b2_sb = sb("b2_sb", [1, H2])
        w3_sb = sb("w3_sb", [P, H2])
        select = sb("select", [NS, NS, P], bf16)
        quot_f = sb("quot_f", [NS, B])
        quot_t = sb("quot_t", [NS, B], bf16)
        quot = sb("quot", [P, TILES, NS])
        rem = sb("rem", [P, TILES, NS])
        mask = sb("mask", [P, TILES, NS, R])
        onehot = sb("onehot", [P, 2, NS, P])
        square = sb("square", [P, BC * P])
        picked = sb("picked", [P, 3, SC, D, R])
        zeros = sb("zeros", [P, D])
        emb = sb("emb", [P, TILES, F, 2 * D])
        cols = sb("cols", [P, 2, QP, F])
        z = sb("z", [P, 2, CH, P])
        ones = sb("ones", [1, P])
        h1 = sb("h1", [P, H1])
        h1t = sb("h1t", [P, H1 // P, P])
        h2w = sb("h2w", [P, H2])
        y = sb("y", [P, TILES])

        gram = ps("gram", [P, Q, 512])
        p1 = ps("p1", [P, H1])
        pt = ps("pt", [P, H1 // P, P])
        psm = ps("psm", [P, 2, 512])

        ids_loaded = sem("ids_loaded")
        ids_t_loaded = sem("ids_t_loaded")
        consts_loaded = sem("consts_loaded")
        tables_loaded = [sem(f"tables_loaded{n}") for n in range(len(TABLE_PARTS))]
        w1_loaded = sem("w1_loaded")
        w2_loaded = sem("w2_loaded")
        ctx_loaded = [sem(f"ctx_loaded{i}") for i in range(2)]
        gathered = [sem(f"gathered{t}") for t in range(TILES)]
        select_ready = sem("select_ready")
        quot_ready = sem("quot_ready")
        z_cleared = sem("z_cleared")
        bcast_made = sem("bcast_made")
        bcast_used = sem("bcast_used")
        onehot_ready = sem("onehot_ready")
        rows_made = sem("rows_made")
        rows_used = sem("rows_used")
        folded = sem("folded")
        zeros_ready = sem("zeros_ready")
        padded = sem("padded")
        z_padded = sem("z_padded")
        cols_ready = sem("cols_ready")
        gram_made = sem("gram_made")
        z_low = sem("z_low")
        z_high = sem("z_high")
        z_used = sem("z_used")
        h1_ready = sem("h1_ready")
        h1t_made = sem("h1t_made")
        h1t_ready = sem("h1t_ready")
        p2_made = sem("p2_made")
        p2_used = sem("p2_used")
        y_ready = sem("y_ready")
        stored = sem("stored")
        act_step = sem("act_step")
        dve_step = sem("dve_step")

        block = ctx.enter_context(nc.Block())

        pt_flat = pt[:].rearrange("p k b -> p (k b)")

        def copy_unit(copy, t, u, h):
            r, qp = divmod(u, Q // 2)
            base = SEG * h
            zt = z[:, t % 2, :, :].rearrange("p c (q j) -> p q j c", q=Q)
            j0 = HALF * h + JU * r
            q = slice(2 * qp, 2 * qp + 2)
            g = gram[:, q, 0:JU * (F - 1)].rearrange("p q (j y) -> p q j y", j=JU)
            copy(zt[0:F, q, j0:j0 + JU, 0:WIDE], g[base:base + F, :, :, QP:QP + WIDE])
            copy(zt[SEG:SEG + QP, q, j0:j0 + JU, 0:QP // 2], g[base:base + QP, :, :, 0:QP:2])
            return copy(zt[SEG + QP:P, q, j0:j0 + JU, 0:QP // 2], g[base:base + QP, :, :, 1:QP:2])

        @block.sync
        def _(sp):
            sp.dma_start(ids_sb[:], ids).then_inc(ids_loaded, 16)
            sp.dma_start(ids_t_sb[:], ids_t).then_inc(ids_t_loaded, 16)
            sp.dma_start(iota[:], iota_in).then_inc(consts_loaded, 16)
            sp.dma_start(ident[:], ident_in).then_inc(consts_loaded, 16)
            for n, (a, b) in enumerate(TABLE_PARTS):
                sp.dma_start(table[:, a:b, :], small.rearrange("p (s c) -> p s c", s=NS)[:, a:b, :]
                             ).then_inc(tables_loaded[n], 16)
            sp.dma_start(w1_sb[:], w1.rearrange("p (c n) -> p c n", c=CH)).then_inc(w1_loaded, 16)
            sp.dma_start(w2_sb[:], w2.rearrange("(k p) n -> p k n", p=P)).then_inc(w2_loaded, 16)
            sp.dma_start(b2_sb[:], b2).then_inc(w2_loaded, 16)
            sp.dma_start(w3_sb[:], w3.to_broadcast([P, H2])).then_inc(w2_loaded, 16)
            sp.wait_ge(z_cleared, 1)
            for t in range(TILES):
                if t >= 2:
                    sp.wait_ge(z_used, t - 1)
                sp.dma_start(z[SEG:SEG + D, t % 2, CH - 1, :], ctx_t[:, t, :]).then_inc(ctx_loaded[t % 2], 16)
            sp.wait_ge(y_ready, TILES)
            sp.dma_start(out.rearrange("(p t) o -> p (t o)", t=TILES), y[:]).then_inc(stored, 16)
            sp.wait_ge(stored, 16)

        @block.gpsimd
        def _(pool):
            pool.wait_ge(ids_loaded, 16)
            for t in range(TILES):
                for s in range(NS, F):
                    nc.gpsimd.indirect_dma_start(
                        emb[:, t, s, 0:D], None, tables[s - NS],
                        bass.IndirectOffsetOnAxis(ap=ids_sb[:, t, s:s + 1], axis=0),
                    ).then_inc(gathered[t], 16)

        @block.scalar
        def _(act):
            act.wait_ge(consts_loaded, 32)
            nc.scalar.activation(select[:], ident[0:NS, 0:NS].unsqueeze(2).to_broadcast([NS, NS, P]),
                                 ACT.Copy).then_inc(select_ready, 1)

            def onehots(t):
                groups = field_groups(BC)
                for u, (a, b) in enumerate(groups):
                    n = NBC * t + u
                    act.wait_ge(bcast_made, n + 1)
                    if n >= 1:
                        act.wait_ge(onehot_ready, n)
                    nc.scalar.activation(square[:, 0:(b - a) * P], pt_flat[:, 0:(b - a) * P], ACT.Square,
                                         bias=iota[:, 1 + R:2 + R]).then_inc(bcast_used, 1)
                    if t >= 2 and u == 0:
                        act.wait_ge(rows_made, NSC * (t - 1))
                    act.wait_ge(bcast_used, n + 1)
                    nc.scalar.activation(onehot[:, t % 2, a:b, :],
                                         square[:, 0:(b - a) * P].rearrange("p (f b) -> p f b", b=P),
                                         ACT.Relu, bias=1.0, scale=-1.0).then_inc(onehot_ready, 1)
                    yield

            def pad(t):
                nc.scalar.copy(emb[:, t, :, D:], zeros[:].unsqueeze(1).to_broadcast([P, F, D])).then_inc(padded, 1)

            def hidden(t):
                act.wait_ge(z_used, t + 1)
                if t >= 1:
                    act.wait_ge(h1t_made, t)
                nc.scalar.activation(h1[:], p1[:], ACT.Relu).then_inc(h1_ready, 1)
                act.wait_ge(h1t_made, t + 1)
                if t >= 1:
                    act.wait_ge(p2_made, t)
                nc.scalar.copy(h1t[:], pt[:]).then_inc(h1t_ready, 1)

            units = itertools.chain.from_iterable(onehots(t) for t in range(TILES))
            act.wait_ge(zeros_ready, 1)
            for _ in range(NBC):
                next(units)
            for t in range(TILES):
                pad(t)
                if t < 2:
                    nc.scalar.copy(z[QP:SEG, t, :, :], zeros[QP:SEG].unsqueeze(1).to_broadcast([QP, CH * P // D, D])
                                   ).then_inc(z_padded, 1)
            for _ in range(broadcasts_sent(2 * NSC) - NBC):
                next(units)
            for t in range(TILES):
                if t >= 2:
                    hidden(t - 2)
                act.wait_ge(z_padded, min(2, t + 1))
                for u in range(UNITS):
                    before = selections_sent(t, u - 1) if u else selections_sent(t - 1, UNITS - 1)
                    for _ in range(broadcasts_sent(selections_sent(t, u)) - broadcasts_sent(before)):
                        next(units)
                    act.wait_ge(gram_made, UNITS * t + u + 1)
                    copy_unit(nc.scalar.copy, t, u, 0).then_inc(z_low, 1)
            hidden(TILES - 2)
            hidden(TILES - 1)

        @block.vector
        def _(dve):
            steps = [0]

            def step(ins):
                steps[0] += 1
                ins.then_inc(dve_step, 1)
                dve.wait_ge(dve_step, steps[0])

            nc.vector.memset(zeros[:], 0.0).then_inc(zeros_ready, 1)
            nc.vector.memset(ones[:], 1.0)
            step(nc.vector.memset(z[SEG:P, :, CH - 1, :], 0.0))
            nc.vector.memset(z[SEG + QP:SEG + QP + 1, :, CH - 1, :], 1.0).then_inc(z_cleared, 1)

            dve.wait_ge(ids_t_loaded, 16)
            step(nc.vector.tensor_scalar(quot_f[:], ids_t_sb[:], -(R - 1) / 2, 1.0 / R, ALU.add, ALU.mult))
            nc.vector.tensor_scalar(quot_t[:], quot_f[:], ROUND, -ROUND, ALU.add, ALU.add).then_inc(quot_ready, 1)
            dve.wait_ge(ids_loaded, 16)
            step(nc.vector.tensor_scalar(quot[:], ids_sb[:, :, 0:NS], -(R - 1) / 2, 1.0 / R, ALU.add, ALU.mult))
            step(nc.vector.tensor_scalar(quot[:], quot[:], ROUND, -ROUND, ALU.add, ALU.add))
            step(nc.vector.scalar_tensor_tensor(rem[:], quot[:], -float(R), ids_sb[:, :, 0:NS],
                                                ALU.mult, ALU.add))
            dve.wait_ge(consts_loaded, 32)
            for t in range(TILES):
                ins = nc.vector.tensor_tensor(mask[:, t], rem[:, t].unsqueeze(2).to_broadcast([P, NS, R]),
                                              iota[:, 1:1 + R].unsqueeze(1).to_broadcast([P, NS, R]),
                                              ALU.is_equal)
            step(ins)

            def fold(t, u):
                m = NSC * t + u
                a, b = field_groups(SC)[u]
                dve.wait_ge(rows_used, m + 1)
                nc.vector.tensor_reduce(emb[:, t, a:b, 0:D], picked[:, m % 3, 0:b - a], AX.X,
                                        ALU.add).then_inc(folded, 1)

            def small_tables(t):
                groups = field_groups(SC)
                for u in range(NSC):
                    m = NSC * t + u
                    a, b = groups[u]
                    k = b - a
                    dve.wait_ge(rows_made, m + 1)
                    if m >= 3:
                        dve.wait_ge(folded, m - 2)
                    nc.vector.tensor_tensor(picked[:, m % 3, 0:k],
                                            psm[:, m % 2, 0:k * R * D].rearrange("p (f r d) -> p f d r", r=R, d=D),
                                            mask[:, t, a:b, :].unsqueeze(2).to_broadcast([P, k, D, R]),
                                            ALU.mult).then_inc(rows_used, 1)
                    if u >= 1:
                        fold(t, u - 1)
                    yield
                fold(t, NSC - 1)

            def columns(t, a, b):
                return nc.vector.transpose(cols[:, t % 2, :, a:b].rearrange("p j s -> p s j"), emb[:, t, a:b, :])

            def last_layer(t):
                if t == 0:
                    dve.wait_ge(w2_loaded, 48)
                dve.wait_ge(p2_made, t + 1)
                nc.vector.scalar_tensor_tensor(h2w[:], psm[:, 0, 0:H2], 0.0, w3_sb[:], ALU.max, ALU.mult,
                                               accum_out=y[:, t:t + 1]).then_inc(y_ready, 1)

            for t in range(2):
                for _ in small_tables(t):
                    pass
            for t in range(TILES):
                small = small_tables(t + 2) if t + 2 < TILES else iter(())
                if t >= 2:
                    dve.wait_ge(gram_made, UNITS * (t - 1))
                dve.wait_ge(folded, NSC * (t + 1))
                dve.wait_ge(padded, t + 1)
                columns(t, 0, NS)
                dve.wait_ge(gathered[t], 16 * NL)
                columns(t, NS, F).then_inc(cols_ready, 1)
                if t >= 2:
                    last_layer(t - 2)
                dve.wait_ge(z_padded, min(2, t + 1))
                for u in range(UNITS):
                    for _ in range(NSC * (u + 1) // UNITS - NSC * u // UNITS):
                        next(small, None)
                    dve.wait_ge(gram_made, UNITS * t + u + 1)
                    copy_unit(nc.vector.tensor_copy, t, u, 1).then_inc(z_high, 1)
                for _ in small:
                    pass
            last_layer(TILES - 2)
            last_layer(TILES - 1)

        @block.tensor
        def _(pe):
            def broadcast_steps():
                for n in range(NBC * TILES):
                    t = n // NBC
                    a, b = field_groups(BC)[n % NBC]
                    if n >= 1:
                        pe.wait_ge(bcast_used, n)
                    for f in range(a, b):
                        ins = nc.tensor.matmul(pt[:, f - a, :], select[:, f, :], quot_t[:, P * t:P * (t + 1)],
                                               start=True, stop=True)
                    ins.then_inc(bcast_made, 1)
                    yield

            broadcasts = broadcast_steps()

            def small_steps(t):
                for u, (a, b) in enumerate(field_groups(SC)):
                    m = NSC * t + u
                    for _ in range(broadcasts_sent(m + 1) - broadcasts_sent(m)):
                        next(broadcasts)
                    if m >= 2:
                        pe.wait_ge(rows_used, m - 1)
                    pe.wait_ge(onehot_ready, NBC * t + -(-b // BC))
                    for n, part in enumerate(TABLE_PARTS):
                        if t == 0 and a == part[0]:
                            pe.wait_ge(tables_loaded[n], 16)
                    for f in range(a, b):
                        k = ROWS[SLOTS[f]] // R
                        ins = nc.tensor.matmul(psm[:, m % 2, (f - a) * R * D:(f - a + 1) * R * D],
                                               onehot[0:k, t % 2, f, :], table[0:k, f, :],
                                               start=True, stop=True)
                    ins.then_inc(rows_made, 1)
                    yield

            def first_layer(t):
                pe.wait_ge(z_low, UNITS * (t + 1))
                pe.wait_ge(z_high, UNITS * (t + 1))
                pe.wait_ge(ctx_loaded[t % 2], 16 * (t // 2 + 1))
                if t == 0:
                    pe.wait_ge(w1_loaded, 16)
                else:
                    pe.wait_ge(h1_ready, t)
                for c in range(CH):
                    ins = nc.tensor.matmul(p1[:], z[:, t % 2, c, :], w1_sb[:, c, :],
                                           start=(c == 0), stop=(c == CH - 1))
                    if c == CH - 1:
                        ins.then_inc(z_used, 1)
                    yield

            def transpose_hidden(t):
                pe.wait_ge(h1_ready, t + 1)
                if t >= 1:
                    pe.wait_ge(h1t_ready, t)
                else:
                    pe.wait_ge(bcast_used, NBC * TILES)
                for k in range(H1 // P):
                    ins = nc.tensor.transpose(pt[:, k, :], h1[:, P * k:P * (k + 1)], ident[:])
                ins.then_inc(h1t_made, 1)

            def second_layer(t):
                if t == 0:
                    pe.wait_ge(w2_loaded, 48)
                    pe.wait_ge(rows_used, NSC * TILES)
                else:
                    pe.wait_ge(y_ready, t)
                nc.tensor.matmul(psm[:, 0, 0:H2], ones[:], b2_sb[:], start=True, stop=False)
                pe.wait_ge(h1t_ready, t + 1)
                for k in range(H1 // P):
                    ins = nc.tensor.matmul(psm[:, 0, 0:H2], h1t[:, k, :], w2_sb[:, k, :],
                                           start=False, stop=(k == H1 // P - 1))
                ins.then_inc(p2_made, 1)

            def gram_products(t):
                pe.wait_ge(cols_ready, t + 1)
                for u in range(UNITS):
                    r, qp = divmod(u, Q // 2)
                    if UNITS * t + u >= 2:
                        pe.wait_ge(z_low, UNITS * t + u - 1)
                        pe.wait_ge(z_high, UNITS * t + u - 1)
                    for jj in range(JU):
                        j = JU * r + jj
                        for q in (2 * qp, 2 * qp + 1):
                            for h in range(2):
                                e = cols[QP * q:QP * q + D, t % 2, HALF * h + j, :]
                                ins = nc.tensor.matmul(
                                    gram[SEG * h:SEG * h + F, q, jj * (F - 1):(jj + 1) * (F - 1)],
                                    e, e[:, 1:F], start=True, stop=True)
                            if jj == JU - 1 and q % 2:
                                ins.then_inc(gram_made, 1)
                            yield

            GROUPS = UNITS * JU * 2

            def share(steps, n, g):
                for _ in range(n * (g + 1) // GROUPS - n * g // GROUPS):
                    next(steps, None)

            pe.wait_ge(select_ready, 1)
            pe.wait_ge(quot_ready, 1)
            pe.wait_ge(consts_loaded, 32)
            pe.wait_ge(z_cleared, 1)
            for t in range(2):
                for _ in small_steps(t):
                    pass
            for t in range(TILES):
                small = small_steps(t + 2) if t + 2 < TILES else iter(())
                layer = first_layer(t - 1) if t >= 1 else iter(())
                lead = LEAD[t]
                for _ in range(lead):
                    next(layer)
                for g, _ in enumerate(gram_products(t)):
                    if t >= 2 and g == 1:
                        transpose_hidden(t - 2)
                    if t >= 2 and g == 7:
                        second_layer(t - 2)
                    share(small, NSC, g)
                    share(layer, CH - lead, g)
                for _ in small:
                    pass
                for _ in layer:
                    pass
            last = first_layer(TILES - 1)
            next(last)
            transpose_hidden(TILES - 2)
            next(last)
            next(last)
            second_layer(TILES - 2)
            for _ in last:
                pass
            transpose_hidden(TILES - 1)
            second_layer(TILES - 1)


def pair_index(i, j):
    return i * (2 * F - i - 1) // 2 + j - i - 1


def weight_rows():
    pairs = F * (F - 1) // 2
    bias, zero = pairs + D, pairs + D + 1
    rows = np.full((P, CH), zero)
    for yy in range(1, F):
        c, p0 = (yy - QP - 1, 0) if yy > QP else ((yy - 1) // 2, SEG + QP * ((yy - 1) % 2))
        for i in range(yy):
            a, b = sorted((SLOTS[i], SLOTS[yy]))
            rows[p0 + i, c] = pair_index(a, b)
    rows[SEG:SEG + D, CH - 1] = pairs + np.arange(D)
    rows[SEG + QP, CH - 1] = bias
    return rows


def kernel(**inputs):
    import concourse.bacc as bacc
    from concourse.bass_utils import run_bass_kernel_spmd

    a = {k: np.asarray(v) for k, v in inputs.items()}
    w1 = np.concatenate([a["W_top1"], a["b_top1"][None], np.zeros((1, H1), np.float32)])
    ids = a["ids"][:, SLOTS]
    packed = [np.concatenate([a[f"tbl_{f}"].reshape(-1, R * D),
                              np.zeros((P - ROWS[f] // R, R * D), np.float32)]) for f in SMALL]
    arrays = {
        "ids": ids.reshape(P, TILES * F),
        "ids_t": ids[:, :NS].reshape(P, TILES, NS).transpose(2, 1, 0).reshape(NS, B),
        "ctx_t": a["dense_ctx"].reshape(P, TILES, D).transpose(2, 1, 0),
        "small": np.stack(packed, 1).reshape(P, NS * R * D),
        "w1": w1[weight_rows()].reshape(P, CH * H1),
        "w2": a["W_top2"],
        "b2": a["b_top2"][None],
        "w3": a["W_top3"].reshape(1, H2),
        "ident": np.eye(P, dtype=np.float32),
        "iota": np.concatenate([np.arange(P)[:, None], np.tile(np.arange(R), (P, 1)), -np.arange(P)[:, None]], 1).astype(np.float32),
    }
    arrays = {f"in_{name}": np.ascontiguousarray(x) for name, x in arrays.items()}
    nc = bacc.Bacc("TRN2", target_bir_lowering=False, num_devices=1)
    args = []
    for name, x in arrays.items():
        args.append(nc.dram_tensor(name, x.shape, mybir.dt.from_np(x.dtype), kind="ExternalInput").ap())
    out = nc.dram_tensor("y_out", (B, 1), mybir.dt.float32, kind="ExternalOutput").ap()
    tabs = []
    for f in LARGE:
        arrays[f"tbl_{f}"] = x = np.ascontiguousarray(a[f"tbl_{f}"])
        tabs.append(nc.dram_tensor(f"tbl_{f}", x.shape, mybir.dt.from_np(x.dtype), kind="ExternalInput").ap())
    args[0] = args[0].rearrange("p (t f) -> p t f", t=TILES)
    build_tower(nc, *args, out, *tabs)
    return run_bass_kernel_spmd(nc, [arrays], core_ids=[0]).results[0]["y_out"]
```

```python
import itertools
from contextlib import ExitStack

import numpy as np

import concourse.bass as bass
from concourse import mybir

P = 128
B = 512
TILES = B // P
F = 50
D = 16
ROWS = [1250, 125000, 125000, 125000, 12500, 125000, 1000, 1250, 125000, 1000, 1000, 125000, 1250,
        1250, 1250, 125000, 1000, 1000, 12500, 125000, 125000, 1250, 1250, 12500, 1250, 12500, 1000,
        1000, 1000, 1250, 1250, 125000, 1250, 1250, 12500, 12500, 125000, 125000, 1250, 1000, 125000,
        12500, 1000, 12500, 1000, 125000, 12500, 1250, 1250, 12500]
R = 10
SMALL = [f for f in range(F) if ROWS[f] <= R * P]
LARGE = [f for f in range(F) if ROWS[f] > R * P]
SLOTS = SMALL + LARGE
NS = len(SMALL)
NL = len(LARGE)
H1 = 512
H2 = 256
Q = 4
QP = P // Q
HALF = QP // 2
SIDE = 64
CH = 12
TOPS = list(range(F - 1, 1, -CH))
STARTS = [sum(TOPS[:k]) for k in range(len(TOPS) + 1)]
STAGED = TOPS[1]
XP = STARTS[-1]
EP = XP + 1
EC = CH // 2
JU = HALF // 2
UNITS = 2 * (Q // 2)
BC = 4
SC = 3
AHEAD = 3
START = [0,16,20,20]
LEFT = [0,4,6,6]
FILLS = len(TOPS) + 1
NBC = -(-NS // BC)
NSC = -(-NS // SC)
ROUND = 1.5 * 2 ** 23


TABLE_PARTS = [(0, SC), (SC, 3 * SC), (3 * SC, 6 * SC), (6 * SC, NS)]


def field_groups(size):
    return [(a, min(a + size, NS)) for a in range(0, NS, size)]


def spread(n, k, parts):
    return -(-n * k // parts)


def broadcasts_sent(n):
    if n == 0:
        return 0
    t, u = divmod(n - 1, NSC)
    return min(NBC * TILES, NBC * t + -(-field_groups(SC)[u][1] // BC) + min(n, AHEAD))


def selections_sent(t, u):
    return min(NSC * TILES, NSC * (t + 2) + spread(NSC, u + 1, UNITS))


def build_tower(nc, ids, ids_t, extra, small, w1, w2, b2, w3, ident_in, iota_in, zeros_in, out, *tables):
    f32 = mybir.dt.float32
    bf16 = mybir.dt.bfloat16
    i32 = mybir.dt.int32
    ALU = mybir.AluOpType
    ACT = mybir.ActivationFunctionType
    AX = mybir.AxisListType

    ctx = ExitStack()
    with ctx:
        def sb(name, shape, dt=f32):
            return ctx.enter_context(nc.sbuf_tensor(name, shape, dt))

        def ps(name, shape):
            return ctx.enter_context(nc.psum_tensor(name, shape, f32))

        def sem(name):
            return ctx.enter_context(nc.semaphore(name))

        ids_sb = sb("ids_sb", [P, TILES, F], i32)
        ids_t_sb = sb("ids_t_sb", [NS, B], i32)
        ident = sb("ident", [P, P])
        iota = sb("iota", [P, 2 + R])
        table = sb("table", [P, NS, R * D])
        table_bf = sb("table_bf", [P, 3, NS, R * D], bf16)
        w1_sb = sb("w1_sb", [P, CH, H1])
        w2_sb = sb("w2_sb", [P, H1 // P, H2])
        b2_sb = sb("b2_sb", [1, H2])
        w3_sb = sb("w3_sb", [P, H2])
        ident_bf = sb("ident_bf", [P, P], bf16)
        quot_f = sb("quot_f", [NS, B])
        quot_t = sb("quot_t", [P, B], bf16)
        quot = sb("quot", [P, TILES, NS])
        rem = sb("rem", [P, TILES, NS])
        mask = sb("mask", [P, TILES, NS, R])
        onehot = sb("onehot", [P, 2, NS, P], bf16)
        square = sb("square", [P, BC * P])
        picked = sb("picked", [P, 3, SC, D, R])
        emb = sb("emb", [P, TILES, F, 2 * D])
        cols = sb("cols", [P, 2, QP, F])
        z = sb("z", [P, 2, CH, P])
        stage = sb("stage", [STAGED, 2, STAGED, P])
        ones = sb("ones", [1, P])
        h1 = sb("h1", [P, H1])
        h1t = sb("h1t", [P, H1 // P, P])
        h2w = sb("h2w", [P, H2])
        y = sb("y", [P, TILES])

        gram = ps("gram", [P, Q, 512])
        p1 = ps("p1", [P, H1])
        pt = ps("pt", [P, H1 // P, P])
        psm = ps("psm", [P, 2, 512])

        ids_loaded = sem("ids_loaded")
        ids_t_loaded = sem("ids_t_loaded")
        consts_loaded = sem("consts_loaded")
        tables_loaded = [sem(f"tables_loaded{n}") for n in range(len(TABLE_PARTS))]
        high_ready = sem("high_ready")
        rest_ready = sem("rest_ready")
        middle_ready = sem("middle_ready")
        low_ready = sem("low_ready")
        w1_loaded = sem("w1_loaded")
        w2_loaded = sem("w2_loaded")
        z_filled = [sem(f"z_filled{i}") for i in range(2)]
        gathered = [sem(f"gathered{t}") for t in range(TILES)]
        selector_ready = sem("selector_ready")
        quot_ready = sem("quot_ready")
        ones_ready = sem("ones_ready")
        bcast_made = sem("bcast_made")
        bcast_used = sem("bcast_used")
        onehot_ready = sem("onehot_ready")
        rows_made = sem("rows_made")
        rows_used = sem("rows_used")
        folded = sem("folded")
        padded = sem("padded")
        z_padded = sem("z_padded")
        cols_ready = sem("cols_ready")
        gram_made = sem("gram_made")
        z_low = sem("z_low")
        z_high = sem("z_high")
        z_used = sem("z_used")
        h1_ready = sem("h1_ready")
        h1t_made = sem("h1t_made")
        h1t_ready = sem("h1t_ready")
        p2_made = sem("p2_made")
        p2_used = sem("p2_used")
        y_ready = sem("y_ready")
        stored = sem("stored")
        act_step = sem("act_step")
        dve_step = sem("dve_step")

        block = ctx.enter_context(nc.Block())

        sums = [p1[:], psm[:, 1, :]]
        pt_flat = pt[:].rearrange("p k b -> p (k b)")

        def copy_unit(copy, t, u, h):
            r, qp = divmod(u, Q // 2)
            base = SIDE * h
            j0 = HALF * h + JU * r
            q = slice(2 * qp, 2 * qp + 2)
            g = gram[:, q, 0:JU * (F - 1)].rearrange("p q (j y) -> p q j y", j=JU)
            staged = stage[:, t % 2, :, :].rearrange("p y (q j) -> p q j y", q=Q)
            copy(staged[:, q, j0:j0 + JU, :], g[base:base + STAGED, :, :, 0:STAGED])
            zt = z[:, t % 2, :, :].rearrange("p c (q j) -> p q j c", q=Q)
            return copy(zt[0:F - 1, q, j0:j0 + JU, :], g[base:base + F - 1, :, :, STAGED:])

        @block.sync
        def _(sp):
            sp.dma_start(ids_sb[:], ids).then_inc(ids_loaded, 16)
            sp.dma_start(ids_t_sb[:], ids_t).then_inc(ids_t_loaded, 16)
            sp.dma_start(iota[:], iota_in).then_inc(consts_loaded, 16)
            sp.dma_start(ident[:], ident_in).then_inc(consts_loaded, 16)
            for n, (a, b) in enumerate(TABLE_PARTS):
                sp.dma_start(table[:, a:b, :], small.rearrange("p (s c) -> p s c", s=NS)[:, a:b, :]
                             ).then_inc(tables_loaded[n], 16)
            sp.dma_start(z[XP:P], zeros_in.rearrange("o (i c b) -> o i c b", i=2, c=CH).to_broadcast([P - XP, 2, CH, P])
                         ).then_inc(z_padded, 16)
            sp.dma_start(w1_sb[:], w1.rearrange("p (c n) -> p c n", c=CH)).then_inc(w1_loaded, 16)
            sp.dma_start(w2_sb[:], w2.rearrange("(k p) n -> p k n", p=P)).then_inc(w2_loaded, 16)
            sp.dma_start(b2_sb[:], b2).then_inc(w2_loaded, 16)
            sp.dma_start(w3_sb[:], w3.to_broadcast([P, H2])).then_inc(w2_loaded, 16)
            sp.wait_ge(z_padded, 16)
            for t in range(TILES):
                if t >= 2:
                    sp.wait_ge(z_used, t - 1)
                sp.dma_start(z[EP:P, t % 2, 0:EC, :], extra[:, :, t, :]).then_inc(z_filled[t % 2], 16)
                sp.wait_ge(z_low, UNITS * (t + 1))
                sp.wait_ge(z_high, UNITS * (t + 1))
                for top, p0 in list(zip(TOPS, STARTS))[1:]:
                    sp.dma_start(z[p0:p0 + top, t % 2, :, :], stage[0:top, t % 2, top - CH:top, :]
                                 ).then_inc(z_filled[t % 2], 16)
                sp.dma_start(z[XP:XP + 1, t % 2, 0, :], stage[0:1, t % 2, 0, :]).then_inc(z_filled[t % 2], 16)
            sp.wait_ge(y_ready, TILES)
            sp.dma_start(out.rearrange("(p t) o -> p (t o)", t=TILES), y[:]).then_inc(stored, 16)
            sp.wait_ge(stored, 16)

        @block.gpsimd
        def _(pool):
            pool.wait_ge(ids_loaded, 16)
            for t in range(TILES):
                for s in range(NS, F):
                    nc.gpsimd.indirect_dma_start(
                        emb[:, t, s, 0:D], None, tables[s - NS],
                        bass.IndirectOffsetOnAxis(ap=ids_sb[:, t, s:s + 1], axis=0),
                    ).then_inc(gathered[t], 16)

        @block.scalar
        def _(act):
            act.wait_ge(consts_loaded, 32)
            nc.scalar.copy(ident_bf[:], ident[:]).then_inc(selector_ready, 1)

            def onehots(t):
                groups = field_groups(BC)
                for u, (a, b) in enumerate(groups):
                    n = NBC * t + u
                    act.wait_ge(bcast_made, n + 1)
                    if n >= 1:
                        act.wait_ge(onehot_ready, n)
                    nc.scalar.activation(square[:, 0:(b - a) * P], pt_flat[:, 0:(b - a) * P], ACT.Square,
                                         bias=iota[:, 1 + R:2 + R]).then_inc(bcast_used, 1)
                    if t >= 2 and u == 0:
                        act.wait_ge(rows_made, NSC * (t - 1))
                    act.wait_ge(bcast_used, n + 1)
                    nc.scalar.activation(onehot[:, t % 2, a:b, :],
                                         square[:, 0:(b - a) * P].rearrange("p (f b) -> p f b", b=P),
                                         ACT.Relu, bias=1.0, scale=-1.0).then_inc(onehot_ready, 1)
                    yield

            def high(n):
                a, b = TABLE_PARTS[n]
                act.wait_ge(tables_loaded[n], 16)
                nc.scalar.copy(table_bf[:, 0, a:b, :], table[:, a:b, :]).then_inc(high_ready, 1)

            def middle(n):
                a, b = TABLE_PARTS[n]
                act.wait_ge(rest_ready, n + 1)
                nc.scalar.copy(table_bf[:, 1, a:b, :], table[:, a:b, :]).then_inc(middle_ready, 1)

            def hidden(t):
                act.wait_ge(z_used, t + 1)
                if t >= 1:
                    act.wait_ge(h1t_made, t)
                nc.scalar.activation(h1[:], sums[t % 2], ACT.Relu).then_inc(h1_ready, 1)
                act.wait_ge(h1t_made, t + 1)
                if t >= 1:
                    act.wait_ge(p2_made, t)
                nc.scalar.copy(h1t[:], pt[:]).then_inc(h1t_ready, 1)

            units = itertools.chain.from_iterable(onehots(t) for t in range(TILES))
            high(0)
            high(1)
            next(units)
            middle(0)
            middle(1)
            next(units)
            high(2)
            next(units)
            middle(2)
            next(units)
            high(3)
            next(units)
            middle(3)
            for n in range(5, broadcasts_sent(2 * NSC)):
                next(units)
            for t in range(TILES):
                for u in range(UNITS):
                    before = selections_sent(t, u - 1) if u else selections_sent(t - 1, UNITS - 1)
                    for _ in range(broadcasts_sent(selections_sent(t, u)) - broadcasts_sent(before)):
                        next(units)
                    act.wait_ge(gram_made, UNITS * t + u + 1)
                    if t >= 2 and u == 0:
                        act.wait_ge(z_used, t - 1)
                    copy_unit(nc.scalar.copy, t, u, 0).then_inc(z_low, 1)
                    if t >= 2 and u == 0:
                        hidden(t - 2)
            hidden(TILES - 2)
            hidden(TILES - 1)

        @block.vector
        def _(dve):
            steps = [0]

            def step(ins):
                steps[0] += 1
                ins.then_inc(dve_step, 1)
                dve.wait_ge(dve_step, steps[0])

            nc.vector.memset(ones[:], 1.0).then_inc(ones_ready, 1)

            def rest(n):
                a, b = TABLE_PARTS[n]
                dve.wait_ge(high_ready, n + 1)
                nc.vector.tensor_tensor(table[:, a:b, :], table[:, a:b, :], table_bf[:, 0, a:b, :],
                                        ALU.subtract).then_inc(rest_ready, 1)

            def low(n):
                a, b = TABLE_PARTS[n]
                dve.wait_ge(middle_ready, n + 1)
                nc.vector.tensor_tensor(table_bf[:, 2, a:b, :], table[:, a:b, :], table_bf[:, 1, a:b, :],
                                        ALU.subtract).then_inc(low_ready, 1)

            step(nc.vector.memset(quot_t[:], 0.0))
            nc.vector.memset(emb[:, :, :, D:], 0.0).then_inc(padded, 1)
            dve.wait_ge(ids_t_loaded, 16)
            step(nc.vector.tensor_scalar(quot_f[:], ids_t_sb[:], -(R - 1) / 2, 1.0 / R, ALU.add, ALU.mult))
            nc.vector.tensor_scalar(quot_t[0:NS, :], quot_f[:], ROUND, -ROUND, ALU.add, ALU.add).then_inc(quot_ready, 1)
            dve.wait_ge(ids_loaded, 16)
            step(nc.vector.tensor_scalar(quot[:], ids_sb[:, :, 0:NS], -(R - 1) / 2, 1.0 / R, ALU.add, ALU.mult))
            step(nc.vector.tensor_scalar(quot[:], quot[:], ROUND, -ROUND, ALU.add, ALU.add))
            step(nc.vector.scalar_tensor_tensor(rem[:], quot[:], -float(R), ids_sb[:, :, 0:NS],
                                                ALU.mult, ALU.add))
            dve.wait_ge(consts_loaded, 32)
            def masks(t):
                return nc.vector.tensor_tensor(mask[:, t], rem[:, t].unsqueeze(2).to_broadcast([P, NS, R]),
                                               iota[:, 1:1 + R].unsqueeze(1).to_broadcast([P, NS, R]),
                                               ALU.is_equal)

            rest(0)
            rest(1)
            step(masks(0))
            low(0)
            low(1)
            rest(2)

            def fold(t, u):
                m = NSC * t + u
                a, b = field_groups(SC)[u]
                dve.wait_ge(rows_used, m + 1)
                nc.vector.tensor_reduce(emb[:, t, a:b, 0:D], picked[:, m % 3, 0:b - a], AX.X,
                                        ALU.add).then_inc(folded, 1)

            def small_tables(t):
                groups = field_groups(SC)
                for u in range(NSC):
                    m = NSC * t + u
                    a, b = groups[u]
                    k = b - a
                    dve.wait_ge(rows_made, m + 1)
                    if m >= 3:
                        dve.wait_ge(folded, m - 2)
                    nc.vector.tensor_tensor(picked[:, m % 3, 0:k],
                                            psm[:, m % 2, 0:k * R * D].rearrange("p (f r d) -> p f d r", r=R, d=D),
                                            mask[:, t, a:b, :].unsqueeze(2).to_broadcast([P, k, D, R]),
                                            ALU.mult).then_inc(rows_used, 1)
                    if u >= 1:
                        fold(t, u - 1)
                    yield
                fold(t, NSC - 1)

            def columns(t, a, b):
                return nc.vector.transpose(cols[:, t % 2, :, a:b].rearrange("p j s -> p s j"), emb[:, t, a:b, :])

            def last_layer(t):
                if t == 0:
                    dve.wait_ge(w2_loaded, 48)
                dve.wait_ge(p2_made, t + 1)
                nc.vector.scalar_tensor_tensor(h2w[:], psm[:, 0, 0:H2], 0.0, w3_sb[:], ALU.max, ALU.mult,
                                               accum_out=y[:, t:t + 1]).then_inc(y_ready, 1)

            def small_columns(t):
                dve.wait_ge(folded, NSC * (t + 1))
                dve.wait_ge(padded, 1)
                columns(t, 0, NS).then_inc(cols_ready, 1)

            def large_columns(t):
                dve.wait_ge(gathered[t], 16 * NL)
                columns(t, NS, F).then_inc(cols_ready, 1)

            for u, _ in enumerate(small_tables(0)):
                if u == 0:
                    low(2)
                elif u == 1:
                    rest(3)
                elif u == 2:
                    low(3)
                    for t in range(1, TILES):
                        ins = masks(t)
                    step(ins)
            for u, _ in enumerate(small_tables(1)):
                if u == 1:
                    small_columns(0)
                elif u == 3:
                    large_columns(0)
            for t in range(TILES):
                small = small_tables(t + 2) if t + 2 < TILES else iter(())
                for u in range(UNITS):
                    for _ in range(spread(NSC, u + 1, UNITS) - spread(NSC, u, UNITS)):
                        next(small, None)
                    dve.wait_ge(gram_made, UNITS * t + u + 1)
                    if t >= 2 and u == 0:
                        dve.wait_ge(z_used, t - 1)
                    copy_unit(nc.vector.tensor_copy, t, u, 1).then_inc(z_high, 1)
                    if t >= 2 and u == 1:
                        last_layer(t - 2)
                    if u == 2 and t + 1 < TILES:
                        if t >= 1:
                            dve.wait_ge(gram_made, UNITS * t)
                        small_columns(t + 1)
                        large_columns(t + 1)
                for _ in small:
                    pass
            last_layer(TILES - 2)
            last_layer(TILES - 1)

        @block.tensor
        def _(pe):
            def broadcast_steps():
                for n in range(NBC * TILES):
                    t = n // NBC
                    a, b = field_groups(BC)[n % NBC]
                    if n >= 1:
                        pe.wait_ge(bcast_used, n)
                    for f in range(a, b):
                        ins = nc.tensor.matmul(pt[:, f - a, :], ident_bf[:, f:f + 1].to_broadcast([P, P]), quot_t[:, P * t:P * (t + 1)],
                                               start=True, stop=True)
                    ins.then_inc(bcast_made, 1)
                    yield

            broadcasts = broadcast_steps()

            def small_steps(t):
                for u, (a, b) in enumerate(field_groups(SC)):
                    m = NSC * t + u
                    for _ in range(broadcasts_sent(m + 1) - broadcasts_sent(m)):
                        next(broadcasts)
                    if m >= 2:
                        pe.wait_ge(rows_used, m - 1)
                    pe.wait_ge(onehot_ready, NBC * t + -(-b // BC))
                    for n, piece in enumerate(TABLE_PARTS):
                        if t == 0 and a == piece[0]:
                            pe.wait_ge(low_ready, n + 1)
                    for f in range(a, b):
                        for part in range(3):
                            ins = nc.tensor.matmul(psm[:, m % 2, (f - a) * R * D:(f - a + 1) * R * D],
                                                   onehot[:, t % 2, f, :], table_bf[:, part, f, :],
                                                   start=(part == 0), stop=(part == 2))
                    ins.then_inc(rows_made, 1)
                    yield

            def first_layer(t):
                pe.wait_ge(z_low, UNITS * (t + 1))
                pe.wait_ge(z_high, UNITS * (t + 1))
                pe.wait_ge(z_filled[t % 2], 16 * FILLS * (t // 2 + 1))
                if t == 0:
                    pe.wait_ge(w1_loaded, 16)
                elif t == 1:
                    pe.wait_ge(rows_used, NSC * TILES)
                else:
                    pe.wait_ge(h1_ready, t - 1)
                for c in range(CH):
                    ins = nc.tensor.matmul(sums[t % 2], z[:, t % 2, c, :], w1_sb[:, c, :],
                                           start=(c == 0), stop=(c == CH - 1))
                    if c == CH - 1:
                        ins.then_inc(z_used, 1)
                    yield

            def transpose_hidden(t):
                pe.wait_ge(h1_ready, t + 1)
                if t >= 1:
                    pe.wait_ge(h1t_ready, t)
                else:
                    pe.wait_ge(bcast_used, NBC * TILES)
                for k in range(H1 // P):
                    ins = nc.tensor.transpose(pt[:, k, :], h1[:, P * k:P * (k + 1)], ident[:])
                ins.then_inc(h1t_made, 1)

            def second_layer(t):
                if t == 0:
                    pe.wait_ge(w2_loaded, 48)
                    pe.wait_ge(rows_used, NSC * TILES)
                else:
                    pe.wait_ge(y_ready, t)
                nc.tensor.matmul(psm[:, 0, 0:H2], ones[:], b2_sb[:], start=True, stop=False)
                pe.wait_ge(h1t_ready, t + 1)
                for k in range(H1 // P):
                    ins = nc.tensor.matmul(psm[:, 0, 0:H2], h1t[:, k, :], w2_sb[:, k, :],
                                           start=False, stop=(k == H1 // P - 1))
                ins.then_inc(p2_made, 1)

            def gram_products(t):
                pe.wait_ge(cols_ready, 2 * (t + 1))
                for u in range(UNITS):
                    r, qp = divmod(u, Q // 2)
                    if UNITS * t + u >= 2:
                        pe.wait_ge(z_low, UNITS * t + u - 1)
                        pe.wait_ge(z_high, UNITS * t + u - 1)
                    for jj in range(JU):
                        j = JU * r + jj
                        for h in range(2):
                            for q in (2 * qp, 2 * qp + 1):
                                side = (h + q) % 2
                                e = cols[QP * q:QP * q + D, t % 2, HALF * side + j, :]
                                ins = nc.tensor.matmul(
                                    gram[SIDE * side:SIDE * side + F, q, jj * (F - 1):(jj + 1) * (F - 1)],
                                    e, e[:, 1:F], start=True, stop=True)
                            if jj == JU - 1 and h == 1:
                                ins.then_inc(gram_made, 1)
                            yield

            GROUPS = UNITS * JU * 2

            def share(steps, n, g, first, end):
                if first <= g < end:
                    for _ in range(spread(n, g + 1 - first, end - first) - spread(n, g - first, end - first)):
                        next(steps, None)

            pe.wait_ge(selector_ready, 1)
            pe.wait_ge(quot_ready, 1)
            pe.wait_ge(consts_loaded, 32)
            pe.wait_ge(ones_ready, 1)
            for t in range(2):
                for _ in small_steps(t):
                    pass
            layers = [first_layer(t) for t in range(TILES)]
            for t in range(TILES):
                small = small_steps(t + 2) if t + 2 < TILES else iter(())
                old = layers[t - 2] if t >= 2 else iter(())
                layer = layers[t - 1] if t >= 1 else iter(())
                for g, _ in enumerate(gram_products(t)):
                    share(small, NSC, g, 0, GROUPS)
                    share(old, LEFT[t - 1], g, 0, START[t])
                    share(layer, CH - LEFT[t], g, START[t], GROUPS)
                    if t >= 2 and g == START[t] + 3:
                        transpose_hidden(t - 2)
                    if t >= 2 and g == START[t] + 11:
                        second_layer(t - 2)
            for _ in layers[TILES - 2]:
                pass
            transpose_hidden(TILES - 2)
            second_layer(TILES - 2)
            for _ in layers[TILES - 1]:
                pass
            transpose_hidden(TILES - 1)
            second_layer(TILES - 1)


def pair_index(i, j):
    return i * (2 * F - i - 1) // 2 + j - i - 1


def weight_rows():
    pairs = F * (F - 1) // 2
    bias, zero = pairs + D, pairs + D + 1
    rows = np.full((P, CH), zero)
    for yy in range(1, F):
        k = next((k for k, top in enumerate(TOPS) if yy > top - CH and yy > 1), len(TOPS))
        c = (yy - 2) % CH if yy > 1 else 0
        p0 = STARTS[k]
        for i in range(yy):
            a, b = sorted((SLOTS[i], SLOTS[yy]))
            rows[p0 + i, c] = pair_index(a, b)
    rows[EP:, :EC] = np.append(pairs + np.arange(D), [bias, zero]).reshape(P - EP, EC)
    return rows


def kernel(**inputs):
    import concourse.bacc as bacc
    from concourse.bass_utils import run_bass_kernel_spmd

    a = {k: np.asarray(v) for k, v in inputs.items()}
    w1 = np.concatenate([a["W_top1"], a["b_top1"][None], np.zeros((1, H1), np.float32)])
    ids = a["ids"][:, SLOTS]
    packed = [np.concatenate([a[f"tbl_{f}"].reshape(-1, R * D),
                              np.zeros((P - ROWS[f] // R, R * D), np.float32)]) for f in SMALL]
    arrays = {
        "ids": ids.reshape(P, TILES * F),
        "ids_t": ids[:, :NS].reshape(P, TILES, NS).transpose(2, 1, 0).reshape(NS, B),
        "extra": np.concatenate([a["dense_ctx"].reshape(P, TILES, D).transpose(2, 1, 0), np.ones((1, TILES, P), np.float32),
                                 np.zeros((1, TILES, P), np.float32)]).reshape(P - EP, EC * B),
        "small": np.stack(packed, 1).reshape(P, NS * R * D),
        "w1": w1[weight_rows()].reshape(P, CH * H1),
        "w2": a["W_top2"],
        "b2": a["b_top2"][None],
        "w3": a["W_top3"].reshape(1, H2),
        "ident": np.eye(P, dtype=np.float32),
        "iota": np.concatenate([np.arange(P)[:, None], np.tile(np.arange(R), (P, 1)), -np.arange(P)[:, None]], 1).astype(np.float32),
        "zeros": np.zeros((1, 2 * CH * P), np.float32),
    }
    arrays = {f"in_{name}": np.ascontiguousarray(x) for name, x in arrays.items()}
    nc = bacc.Bacc("TRN2", target_bir_lowering=False, num_devices=1)
    args = []
    for name, x in arrays.items():
        args.append(nc.dram_tensor(name, x.shape, mybir.dt.from_np(x.dtype), kind="ExternalInput").ap())
    out = nc.dram_tensor("y_out", (B, 1), mybir.dt.float32, kind="ExternalOutput").ap()
    tabs = []
    for f in LARGE:
        arrays[f"tbl_{f}"] = x = np.ascontiguousarray(a[f"tbl_{f}"])
        tabs.append(nc.dram_tensor(f"tbl_{f}", x.shape, mybir.dt.from_np(x.dtype), kind="ExternalInput").ap())
    args[2] = args[2].rearrange("p (c t b) -> p c t b", c=EC, t=TILES)
    args[0] = args[0].rearrange("p (t f) -> p t f", t=TILES)
    build_tower(nc, *args, out, *tabs)
    return run_bass_kernel_spmd(nc, [arrays], core_ids=[0]).results[0]["y_out"]
```
